# Optimizing a Trainium2 kernel written in Bass

```python
import numpy as np
import jax
import jax.numpy as jnp

def _softmax(x, axis=-1):
    return jax.nn.softmax(x, axis=axis)

def _gelu(x):
    return jax.nn.gelu(x, approximate=True)

def _silu(x):
    return jax.nn.silu(x)

def _sigmoid(x):
    return jax.nn.sigmoid(x)

def _layernorm(x, axis=-1, eps=1e-05):
    m = jnp.mean(x, axis=axis, keepdims=True)
    v = jnp.var(x, axis=axis, keepdims=True)
    return (x - m) / jnp.sqrt(v + eps)

def _scatter_add(tgt, idx, src, axis=0):
    return tgt.at[idx].add(src)

def _segment_sum(src, seg, n):
    return jax.ops.segment_sum(src, seg, n)
kernel_name = 'mk_adj_resnorm_d1_adj_r2_92b42a'

def setup_inputs(seed: int=0):
    np.random.seed(seed)
    _w = jnp.asarray

    def _rec_inputs():
        import jax
        import jax.numpy as jnp
        _gk = jax.random.key(seed)
        x = -0.000125 + 0.9999 * jax.random.normal(jax.random.fold_in(_gk, 1), (32, 256, 128), jnp.float32)
        _a = jax.random.bernoulli(jax.random.fold_in(_gk, 2), 0.0625, (256, 256))
        _a = jnp.logical_or(_a, jnp.swapaxes(_a, -1, -2))
        _a = jnp.logical_or(_a, jnp.eye(256, dtype=bool))
        _af = _a.astype(jnp.float32)
        _af = _af * jax.random.uniform(jax.random.fold_in(_gk, 3), (256, 256), jnp.float32, 0.05, 0.999837)
        adj = _af
        return (x, adj)
    x, adj = _rec_inputs()

    def _L0_gnn_setup():
        import jax, jax.numpy as jnp
        import numpy as np
        NEG = -9000000000000000.0
        key = jax.random.key(seed)
        k1, k2, k3, k4 = jax.random.split(key, 4)
        B, N, F_in, F_out, MAX_E = (8192, 16, 128, 128, 128)
        inp = jax.random.normal(k1, (B, N, F_in), dtype=jnp.float32)
        adj = jax.random.uniform(k2, (N, N), dtype=jnp.float32)
        limit = 1.414 * np.sqrt(6.0 / (F_in + F_out))
        W = jax.random.uniform(k3, (2, F_in, F_out), dtype=jnp.float32, minval=-limit, maxval=limit)
        e = jnp.ones((1, MAX_E), dtype=jnp.float32)
        stdv = 1.0 / np.sqrt(F_out)
        bias = jax.random.uniform(k4, (F_out,), dtype=jnp.float32, minval=-stdv, maxval=stdv)
        return {'input': inp, 'adj': adj, 'W': W, 'e': e, 'bias': bias}
    _L0_gnn_all = _L0_gnn_setup()
    _L0_gnn_in = {k: v for k, v in _L0_gnn_all.items() if k in ('W', 'e', 'bias')}
    del _L0_gnn_all
    return {'x': x, 'adj': adj, 'L0_gnn_W': _L0_gnn_in['W'], 'L0_gnn_e': _L0_gnn_in['e'], 'L0_gnn_bias': _L0_gnn_in['bias']}

def reference(x, adj, L0_gnn_W, L0_gnn_e, L0_gnn_bias):
    import jax
    import jax.numpy as jnp

    def _L0_gnn_ref(input, adj, W, e, bias):
        import jax, jax.numpy as jnp
        import numpy as np
        NEG = -9000000000000000.0
        h0 = jnp.einsum('bnf,fg->bng', input, W[0])
        h1 = jnp.einsum('bnf,fg->bng', input, W[1])
        m = adj > 0
        idx = jnp.cumsum(m.reshape(-1).astype(jnp.int32)) - 1
        vals = e[0][idx].reshape(adj.shape)
        A = jnp.where(m, vals, jnp.float32(NEG))
        A = jax.nn.softmax(A, axis=1)
        M = jnp.eye(adj.shape[0], dtype=A.dtype)
        out = jnp.einsum('ij,bjg->big', A * M, h0) + jnp.einsum('ij,bjg->big', A * (1.0 - M), h1)
        return out + bias[None, None, :]
    x = _layernorm(x + _L0_gnn_ref(x, adj, L0_gnn_W, L0_gnn_e, L0_gnn_bias), axis=-1)
    return x

_drawn_inputs = setup_inputs


def setup_inputs(seed=0):
    import zlib

    import numpy as np

    out = dict(_drawn_inputs(seed))
    spreads = {'L0_gnn_e': (1.0, 0.6)}
    factors = {}
    for name, (base, spread) in spreads.items():
        noise = np.random.default_rng([zlib.crc32(name.encode()), seed]).standard_normal(out[name].shape)
        drawn = base * np.exp(spread * noise) if base else spread * noise
        out[name] = jnp.asarray(drawn.astype(out[name].dtype))
    for name, factor in factors.items():
        out[name] = (out[name] * factor).astype(out[name].dtype)
    return out
```

```python
import concourse.bass as bass
from concourse import mybir
from contextlib import ExitStack

fp32 = mybir.dt.float32
bf16 = mybir.dt.bfloat16
ALU = mybir.AluOpType
ACT = mybir.ActivationFunctionType
AX = mybir.AxisListType

P = 128
NEG = 9000000000000000.0
EPS = 1e-5
RING = 4


def gnn_resnorm_kernel(nc, x, adj, W, e, bias, out):
    B, N, F = x.shape
    T = N // P
    GB = 2
    NG = B // GB
    ROUNDS = NG // RING
    C = GB * F
    GC = T * C
    E = e.shape[1]
    CAP = 200

    x_v = x.rearrange("(n b) (p t) f -> n p b t f", b=GB, t=T)
    out_v = out.rearrange("(n b) (p t) f -> n p b t f", b=GB, t=T)

    ctx = ExitStack()
    with ctx:
        def sb(name, shape, dt=fp32):
            return ctx.enter_context(nc.sbuf_tensor(name, shape, dt))

        def ps(name, shape, dt=fp32):
            return ctx.enter_context(nc.psum_tensor(name, shape, dt))

        def sem(name):
            return ctx.enter_context(nc.semaphore(name))

        ident = sb("ident", [P, P])
        ident_b = sb("ident_b", [P, P], bf16)
        before = sb("before", [P, P])
        rank_row = sb("rank_row", [P, E])
        rank1_col = sb("rank1_col", [P, 1])
        w_sb = sb("w_sb", [P, 2, F])
        bias_sb = sb("bias_sb", [P, 1, F])
        e_col = sb("e_col", [P, 1])
        e_last = sb("e_last", [P, 1])
        adj_sb = sb("adj_sb", [P, T * N])
        mask = sb("mask", [P, T * N])
        count = sb("count", [P, T * N])
        local = sb("local", [P, T * N], bf16)
        first = sb("first", [P, 1])
        first_b = sb("first_b", [P, 1], bf16)
        end = sb("end", [P, 1])
        thr = sb("thr", [P, 1])
        begun = sb("begun", [P, E])
        owner_t = sb("owner_t", [P, E], bf16)
        owner = sb("owner", [P, P])
        want = sb("want", [P, 1])
        placed = sb("placed", [P, T * N])
        late = sb("late", [P, T * N])
        neg = sb("neg", [P, T * N])
        logit = sb("logit", [P, T, N])
        rowmax = sb("rowmax", [P, T])
        negmax = sb("negmax", [P, T])
        prob = sb("prob", [P, T, N])
        rowsum = sb("rowsum", [P, T])
        rinv = sb("rinv", [P, T])
        diag_m = sb("diag_m", [P, T, P])
        a_diag = sb("a_diag", [P, T])
        at = sb("at", [P, T, T, P])
        xs = [sb(f"xs{k}", [P, GB, T, F]) for k in range(RING)]
        res = [sb(f"res{k}", [P, GB, T, F]) for k in range(RING)]
        ys = [sb(f"ys{k}", [P, GB, T, F]) for k in range(RING)]
        xt = [sb(f"xt{k}", [P, GB, T, P]) for k in range(2)]
        h1 = [sb(f"h1_{k}", [P, T, GB, F]) for k in range(2)]
        ts = [sb(f"ts{k}", [P, T, GB, F]) for k in range(2)]
        stats = [sb(f"stats{k}", [P, T * GB, 6]) for k in range(2)]
        mv = [sb(f"mv{k}", [P, T * GB, 2]) for k in range(2)]
        std = [sb(f"std{k}", [P, T * GB]) for k in range(2)]
        rstd = [sb(f"rstd{k}", [P, T * GB]) for k in range(2)]
        nmr = [sb(f"nmr{k}", [P, T * GB]) for k in range(2)]
        eps_c = sb("eps_c", [P, 1])

        ps_x = [ps(f"ps_x{k}", [P, GB, T, P]) for k in range(2)]
        ps_h0 = [ps(f"ps_h0{k}", [P, T, GB, F]) for k in range(2)]
        ps_h1 = [ps(f"ps_h1{k}", [P, T, GB, F]) for k in range(2)]
        ps_o = [ps(f"ps_o{k}", [P, T, GB, F]) for k in range(2)]
        so = [t[:, :, :, :].rearrange("p t b f -> p (t b f)") for t in ps_o]
        owner_ps = so[1][:, 128:192].bitcast(bf16)

        x_in = [sem(f"x_in{k}") for k in range(RING)]
        y_stored = [sem(f"y_stored{k}") for k in range(RING)]
        adj_in, w_in, bias_in, e_in = sem("adj_in"), sem("w_in"), sem("bias_in"), sem("e_in")
        zeroed, consts = sem("zeroed"), sem("consts")
        mask_ok, count_ok, local_ok = sem("mask_ok"), sem("count_ok"), sem("local_ok")
        first_ps_ok, first_ok, thr_ok = sem("first_ps_ok"), sem("first_ok"), sem("thr_ok")
        begun_ok, owner_t_ok, owner_ps_ok = sem("begun_ok"), sem("owner_t_ok"), sem("owner_ps_ok")
        owner_ok, want_ok, placed_ok, sparse_ok = sem("owner_ok"), sem("want_ok"), sem("placed_ok"), sem("sparse_ok")
        neg_ok, late_ok, logit_ok = sem("neg_ok"), sem("late_ok"), sem("logit_ok")
        max_ok, exp_ok, rinv_ok, prob_ok = sem("max_ok"), sem("exp_ok"), sem("rinv_ok"), sem("prob_ok")
        diag_ok, off_ok, at_ps_ok, at_ok = sem("diag_ok"), sem("off_ok"), sem("at_ps_ok"), sem("at_ok")
        xt_done, xt_ready = sem("xt_done"), sem("xt_ready")
        h_done, h1_ready = sem("h_done"), sem("h1_ready")
        biased, resid = sem("biased"), sem("resid")
        mixed, summed = sem("mixed"), sem("summed")
        bn_done, var_ok, std_ok, rstd_ok, nmr_ok = sem("bn_done"), sem("var_ok"), sem("std_ok"), sem("rstd_ok"), sem("nmr_ok")
        norm_v, norm_s = sem("norm_v"), sem("norm_s")

        block = ctx.enter_context(nc.Block())

        def loads_then_stores(sp):
            def load(g, k, again):
                if again:
                    sp.wait_ge(xt_done, g - RING + 1)
                    sp.wait_ge(biased, g - RING + 1)
                sp.dma_start(xs[k][:, :, :, :], x_v[g]).then_inc(x_in[k], 16)

            def store(g, k):
                sp.wait_ge(norm_v, g + 1)
                sp.wait_ge(norm_s, g + 1)
                sp.dma_start(out_v[g], ys[k][:, :, :, :]).then_inc(y_stored[k], 16)

            sp.dma_start(adj_sb[:, :], adj.rearrange("(p t) j -> p (t j)", t=T)).then_inc(adj_in, 16)
            for k in range(RING):
                load(k, k, False)
            for k in range(RING):
                load(RING + k, k, True)
            with sp.Fori(1, ROUNDS - 1) as r:
                g = r * RING
                for k in range(RING):
                    load(g + (RING + k), k, True)
                    store(g + (k - RING), k)
            for g in range(NG - 2 * RING, NG):
                store(g, g % RING)
            for k in range(RING):
                sp.wait_ge(y_stored[k], 16 * (NG // RING))

        @block.sync
        def _(sp):
            loads_then_stores(sp)

        @block.gpsimd
        def _(pool):
            pool.memset(ident[:, :], 0.0).then_inc(zeroed, 1)
            pool.memset(before[:, :], 0.0).then_inc(zeroed, 1)
            pool.iota(rank_row[:, :], pattern=[[1, E]], base=0, channel_multiplier=0,
                      allow_small_or_imprecise_dtypes=True).then_inc(consts, 1)
            pool.iota(rank1_col[:, :], pattern=[[1, 1]], base=1, channel_multiplier=1,
                      allow_small_or_imprecise_dtypes=True).then_inc(consts, 1)
            pool.memset(eps_c[:, :], EPS).then_inc(consts, 1)
            pool.wait_ge(zeroed, 2)
            pool.affine_select(out=ident[:, :], in_=ident[:, :], compare_op=ALU.not_equal, fill=1.0,
                               base=0, pattern=[[-1, P]], channel_multiplier=1).then_inc(consts, 1)
            pool.affine_select(out=before[:, :], in_=before[:, :], compare_op=ALU.is_ge, fill=1.0,
                               base=0, pattern=[[-1, P]], channel_multiplier=1).then_inc(consts, 1)
            pool.wait_ge(consts, 5)
            pool.tensor_copy(ident_b[:, :], ident[:, :]).then_inc(consts, 1)

            bias_bc = bias_sb[:, :, :].broadcast_to([P, GB * T, F])

            def add_bias(g, k, again):
                if again:
                    pool.wait_ge(summed, g - RING + 1)
                    pool.wait_ge(x_in[k], (g - k) * (16 // RING) + 16)
                else:
                    pool.wait_ge(x_in[k], 16)
                pool.tensor_tensor(res[k][:, :, :, :].rearrange("p b t f -> p (b t) f"),
                                   xs[k][:, :, :, :].rearrange("p b t f -> p (b t) f"),
                                   bias_bc, ALU.add).then_inc(biased, 1)

            pool.wait_ge(bias_in, 16)
            for k in range(RING):
                add_bias(k, k, False)
            with pool.Fori(1, ROUNDS) as r:
                g = r * RING
                for k in range(RING):
                    add_bias(g + k, k, True)

        @block.scalar
        def _(act):
            act.dma_start(e_col[:, :], e.rearrange("a k -> k a")).then_inc(e_in, 16)
            act.dma_start(e_last[:, :], e[0:1, E - 1:E].broadcast_to([P, 1])).then_inc(e_in, 16)
            act.dma_start(w_sb[:, :, :], W.rearrange("w f g -> f w g")).then_inc(w_in, 16)
            act.dma_start(bias_sb[:, 0, :], bias.rearrange("(a f) -> a f", a=1).broadcast_to([P, F])).then_inc(bias_in, 16)

            def evac_xt(g, k, warm):
                act.wait_ge(xt_done, g + 1)
                if warm:
                    act.wait_ge(h_done, g - 1)
                act.activation(xt[k % 2][:, :, :, :], ps_x[k % 2][:, :, :, :], ACT.Copy).then_inc(xt_ready, 1)

            def evac_h1(g, k, warm):
                act.wait_ge(h_done, g + 1)
                if warm:
                    act.wait_ge(mixed, g - 1)
                act.activation(h1[k % 2][:, :, :, :], ps_h1[k % 2][:, :, :, :], ACT.Copy).then_inc(h1_ready, 1)

            def norm_part(g, k, warm):
                act.wait_ge(nmr_ok, g + 1)
                if warm:
                    act.wait_ge(y_stored[k], (g - k) * (16 // RING))
                for b in range(GB):
                    j = b
                    ins = act.activation(ys[k][:, b, 0, :], ts[k % 2][:, 0, b, :], ACT.Identity,
                                         bias=nmr[k % 2][:, j:j + 1], scale=rstd[k % 2][:, j:j + 1])
                ins.then_inc(norm_s, 1)

            def sqrt_var(g, k, warm):
                act.wait_ge(var_ok, g + 1)
                if warm:
                    act.wait_ge(rstd_ok, g - 1)
                act.activation(std[k % 2][:, :], mv[k % 2][:, :, 1], ACT.Sqrt,
                               bias=eps_c[:, :], scale=1.0).then_inc(std_ok, 1)

            evac_xt(0, 0, False)
            evac_xt(1, 1, False)
            evac_h1(0, 0, False)
            for t in range(T):
                act.wait_ge(max_ok, 2)
                act.activation(prob[:, t, :], logit[:, t, :], ACT.Exp, bias=negmax[:, t:t + 1], scale=1.0,
                               accum_out=rowsum[:, t:t + 1]).then_inc(exp_ok, 1)
            act.wait_ge(consts, 3)
            for s in range(2, 2 * RING):
                evac_xt(s, s % RING, True)
                evac_h1(s - 1, (s - 1) % RING, s > 2)
                if s >= RING:
                    norm_part(s - 4, s % RING, False)
                if s >= 3:
                    sqrt_var(s - 3, (s - 3) % RING, s > 4)
            with act.Fori(2, ROUNDS) as r:
                g = r * RING
                for k in range(RING):
                    evac_xt(g + k, k, True)
                    evac_h1(g + (k - 1), (k - 1) % RING, True)
                    norm_part(g + (k - 4), k, True)
                    sqrt_var(g + (k - 3), (k - 3) % RING, True)
            evac_h1(NG - 1, RING - 1, True)
            for g in range(NG - 4, NG):
                norm_part(g, g % RING, True)
                if g + 1 < NG:
                    sqrt_var(g + 1, (g + 1) % RING, True)

        @block.tensor
        def _(pe):
            def transposes(g, k, loaded, warm):
                pe.wait_ge(x_in[k], loaded)
                if warm:
                    pe.wait_ge(xt_ready, g - 1)
                for b in range(GB):
                    for t in range(T):
                        ins = pe.transpose(ps_x[k % 2][:, b, t, :], xs[k][:, b, t, :], ident[:, :])
                ins.then_inc(xt_done, 1)

            def products(g, k, warm):
                pe.wait_ge(xt_ready, g + 1)
                if warm:
                    pe.wait_ge(resid, g - 1)
                    pe.wait_ge(h1_ready, g - 1)
                for b in range(GB):
                    for t in range(T):
                        pe.matmul(ps_h1[k % 2][:, t, b, :], xt[k % 2][:, b, t, :], w_sb[:, 1, :], start=True, stop=True)
                        ins = pe.matmul(ps_h0[k % 2][:, t, b, :], xt[k % 2][:, b, t, :], w_sb[:, 0, :], start=True, stop=True)
                ins.then_inc(h_done, 1)

            def mix(g, k, warm):
                pe.wait_ge(h1_ready, g + 1)
                if warm:
                    pe.wait_ge(summed, g - 1)
                for t in range(T):
                    for s in range(T):
                        ins = pe.matmul(ps_o[k % 2][:, t, :, :], at[:, s, t, :], h1[k % 2][:, s, :, :],
                                        start=(s == 0), stop=(s == T - 1))
                ins.then_inc(mixed, 1)

            pe.wait_ge(consts, 6)
            transposes(0, 0, 16, False)
            pe.wait_ge(count_ok, 1)
            pe.matmul(so[0][:, 0:1], before[:, :], count[:, T * N - 1:T * N], start=True, stop=True).then_inc(first_ps_ok, 1)
            transposes(1, 1, 16, False)
            pe.wait_ge(w_in, 16)
            products(0, 0, False)
            pe.wait_ge(owner_t_ok, 1)
            pe.transpose(owner_ps, owner_t[:, :], ident_b[:, :]).then_inc(owner_ps_ok, 1)
            pe.wait_ge(first_ok, 3)
            pe.matmul(so[1][:, 0:1], owner_t[:, :], first_b[:, :], start=True, stop=True).then_inc(owner_ps_ok, 1)
            pe.wait_ge(local_ok, 1)
            pe.matmul(so[0][:, :], owner_t[:, :], local[:, :], start=True, stop=True).then_inc(owner_ps_ok, 1)
            products(1, 1, False)
            pe.wait_ge(owner_ok, 1)
            pe.wait_ge(placed_ok, 1)
            pe.matmul(so[1][:, :], owner[:, :], placed[:, :], start=True, stop=True).then_inc(sparse_ok, 1)
            pe.wait_ge(off_ok, T)
            for s in range(T):
                for t in range(T):
                    ins = pe.transpose(so[0][:, (s * T + t) * P:(s * T + t + 1) * P], prob[:, t, s:N:T], ident[:, :])
            ins.then_inc(at_ps_ok, 1)
            pe.wait_ge(at_ok, 1)
            for s in range(2, RING):
                transposes(s, s, 16, True)
                if s > 2:
                    products(s - 1, s - 1, True)
                mix(s - 2, s - 2, False)
            with pe.Fori(1, ROUNDS) as r:
                g = r * RING
                for k in range(RING):
                    transposes(g + k, k, g * (16 // RING) + 16, True)
                    products(g + (k - 1), (k - 1) % RING, True)
                    mix(g + (k - 2), (k - 2) % RING, True)
            products(NG - 1, RING - 1, True)
            mix(NG - 2, RING - 2, True)
            mix(NG - 1, RING - 1, True)

        @block.vector
        def _(dve):
            dve.wait_ge(adj_in, 16)
            dve.tensor_scalar(mask[:, :], adj_sb[:, :], 0.0, None, ALU.is_gt).then_inc(mask_ok, 1)
            dve.wait_ge(mask_ok, 1)
            dve.tensor_tensor_scan(count[:, :], mask[:, :], mask[:, :], 0.0, ALU.add, ALU.max).then_inc(count_ok, 1)
            dve.wait_ge(count_ok, 1)
            dve.scalar_tensor_tensor(local[:, :], count[:, :], float(CAP), mask[:, :], ALU.min, ALU.mult).then_inc(local_ok, 1)
            dve.wait_ge(first_ps_ok, 1)
            dve.tensor_copy(first[:, :], so[0][:, 0:1]).then_inc(first_ok, 1)
            dve.wait_ge(first_ok, 1)
            dve.tensor_tensor(end[:, :], first[:, :], count[:, T * N - 1:T * N], ALU.add).then_inc(first_ok, 1)
            dve.tensor_scalar(begun[:, :], rank_row[:, :], first[:, :], None, ALU.is_ge).then_inc(begun_ok, 1)
            dve.tensor_copy(first_b[:, :], first[:, :]).then_inc(first_ok, 1)
            dve.tensor_scalar(thr[:, :], first[:, :], -1.0, float(E), ALU.mult, ALU.add).then_inc(thr_ok, 1)
            dve.wait_ge(first_ok, 3)
            dve.wait_ge(begun_ok, 1)
            dve.scalar_tensor_tensor(owner_t[:, :], rank_row[:, :], end[:, :], begun[:, :], ALU.is_lt, ALU.mult).then_inc(owner_t_ok, 1)
            dve.tensor_scalar(neg[:, :], mask[:, :], NEG, -NEG, ALU.mult, ALU.add).then_inc(neg_ok, 1)
            dve.wait_ge(thr_ok, 1)
            dve.wait_ge(e_in, 32)
            dve.tensor_scalar(late[:, :], count[:, :], thr[:, :], e_last[:, :], ALU.is_gt, ALU.mult).then_inc(late_ok, 1)
            dve.wait_ge(owner_ps_ok, 3)
            dve.tensor_tensor(want[:, :], rank1_col[:, :], so[1][:, 0:1], ALU.subtract).then_inc(want_ok, 1)
            dve.tensor_copy(owner[:, :], owner_ps).then_inc(owner_ok, 1)
            dve.wait_ge(want_ok, 1)
            dve.tensor_scalar(placed[:, :], so[0][:, :], want[:, :], e_col[:, :], ALU.is_equal, ALU.mult).then_inc(placed_ok, 1)
            dve.wait_ge(late_ok, 1)
            dve.tensor_tensor(late[:, :], late[:, :], mask[:, :], ALU.mult).then_inc(late_ok, 1)
            dve.wait_ge(late_ok, 2)
            dve.wait_ge(neg_ok, 1)
            dve.tensor_tensor(late[:, :], late[:, :], neg[:, :], ALU.add).then_inc(late_ok, 1)
            dve.wait_ge(late_ok, 3)
            dve.wait_ge(sparse_ok, 1)
            dve.tensor_tensor(logit[:, :, :].rearrange("p t n -> p (t n)"), so[1][:, :], late[:, :], ALU.add).then_inc(logit_ok, 1)
            dve.wait_ge(logit_ok, 1)
            dve.tensor_reduce(rowmax[:, :], logit[:, :, :], AX.X, ALU.max).then_inc(max_ok, 1)
            dve.wait_ge(max_ok, 1)
            dve.tensor_scalar(negmax[:, :], rowmax[:, :], -1.0, None, ALU.mult).then_inc(max_ok, 1)
            dve.wait_ge(exp_ok, T)
            dve.reciprocal(rinv[:, :], rowsum[:, :]).then_inc(rinv_ok, 1)
            dve.wait_ge(rinv_ok, 1)
            for t in range(T):
                dve.tensor_scalar(prob[:, t, :], prob[:, t, :], rinv[:, t:t + 1], None, ALU.mult).then_inc(prob_ok, 1)
            dve.wait_ge(consts, 6)
            for t in range(T):
                dve.wait_ge(prob_ok, t + 1)
                dve.scalar_tensor_tensor(diag_m[:, t, :], prob[:, t, t:N:T], 1.0, ident[:, :], ALU.mult, ALU.mult,
                                         accum_out=a_diag[:, t:t + 1]).then_inc(diag_ok, 1)
            for t in range(T):
                dve.wait_ge(diag_ok, t + 1)
                dve.tensor_tensor(prob[:, t, t:N:T], prob[:, t, t:N:T], diag_m[:, t, :], ALU.subtract).then_inc(off_ok, 1)
            dve.wait_ge(at_ps_ok, 1)
            dve.tensor_copy(at[:, :, :, :].rearrange("p s t n -> p (s t n)"), so[0][:, :]).then_inc(at_ok, 1)

            def residual(g, k):
                dve.wait_ge(h_done, g + 1)
                dve.wait_ge(biased, g + 1)
                for t in range(T):
                    ins = dve.scalar_tensor_tensor(res[k][:, :, t, :], ps_h0[k % 2][:, t, :, :], a_diag[:, t:t + 1],
                                                   res[k][:, :, t, :], ALU.mult, ALU.add)
                ins.then_inc(resid, 1)

            def add_mixed(g, k, warm):
                dve.wait_ge(mixed, g + 1)
                dve.wait_ge(resid, g + 1)
                if warm:
                    dve.wait_ge(norm_v, g - 1)
                    dve.wait_ge(norm_s, g - 1)
                dve.tensor_tensor(ts[k % 2][:, :, :, :], ps_o[k % 2][:, :, :, :],
                                  res[k][:, :, :, :].rearrange("p b t f -> p t b f"), ALU.add).then_inc(summed, 1)

            def statistics(g, k):
                dve.wait_ge(summed, g + 1)
                for t in range(T):
                    for b in range(GB):
                        ins = dve.bn_stats(stats[k % 2][:, t * GB + b, :], ts[k % 2][:, t, b, :])
                ins.then_inc(bn_done, 1)

            def aggregate(g, k):
                for j in range(T * GB):
                    ins = dve.bn_aggr(mv[k % 2][:, j, :], stats[k % 2][:, j, :])
                ins.then_inc(var_ok, 1)

            def invert(g, k):
                dve.wait_ge(std_ok, g + 1)
                dve.reciprocal(rstd[k % 2][:, :], std[k % 2][:, :]).then_inc(rstd_ok, 1)

            def normalise(g, k, warm):
                dve.wait_ge(rstd_ok, g + 1)
                dve.scalar_tensor_tensor(nmr[k % 2][:, :], mv[k % 2][:, :, 0], -1.0, rstd[k % 2][:, :],
                                         ALU.mult, ALU.mult).then_inc(nmr_ok, 1)
                if warm:
                    dve.wait_ge(y_stored[k], (g - k) * (16 // RING))
                for t in range(1, T):
                    for b in range(GB):
                        j = t * GB + b
                        ins = dve.tensor_scalar(ys[k][:, b, t, :], ts[k % 2][:, t, b, :], mv[k % 2][:, j, 0:1],
                                                rstd[k % 2][:, j:j + 1], ALU.subtract, ALU.mult)
                ins.then_inc(norm_v, 1)

            dve.wait_ge(diag_ok, T)
            residual(0, 0)
            residual(1, 1)
            add_mixed(0, 0, False)
            statistics(0, 0)
            dve.wait_ge(bn_done, 1)
            residual(2, 2)
            aggregate(0, 0)
            for s in range(RING, 2 * RING):
                k = s % RING
                add_mixed(s - 3, (s - 3) % RING, s > 4)
                statistics(s - 3, (s - 3) % RING)
                dve.wait_ge(bn_done, s - 2)
                invert(s - 4, k)
                aggregate(s - 3, (s - 3) % RING)
                normalise(s - 4, k, False)
                residual(s - 1, (s - 1) % RING)
            with dve.Fori(2, ROUNDS) as r:
                g = r * RING
                for k in range(RING):
                    add_mixed(g + (k - 3), (k - 3) % RING, True)
                    statistics(g + (k - 3), (k - 3) % RING)
                    dve.wait_ge(bn_done, g + (k - 2))
                    invert(g + (k - 4), k)
                    aggregate(g + (k - 3), (k - 3) % RING)
                    normalise(g + (k - 4), k, True)
                    residual(g + (k - 1), (k - 1) % RING)
            for s in range(NG, NG + 4):
                if s - 3 < NG:
                    add_mixed(s - 3, (s - 3) % RING, True)
                    statistics(s - 3, (s - 3) % RING)
                    dve.wait_ge(bn_done, s - 2)
                invert(s - 4, s % RING)
                if s - 3 < NG:
                    aggregate(s - 3, (s - 3) % RING)
                normalise(s - 4, s % RING, True)
                if s == NG:
                    residual(NG - 1, RING - 1)


_INS = ['x', 'adj', 'L0_gnn_W', 'L0_gnn_e', 'L0_gnn_bias']
_OUTS = [((32, 256, 128), 'float32')]


def kernel(**inputs):
    import numpy as _np
    import concourse.bacc as _bacc
    from concourse import mybir as _mybir
    from concourse.bass_utils import run_bass_kernel_spmd as _run

    nc = _bacc.Bacc("TRN2", target_bir_lowering=False, num_devices=1)
    arrays, args = {}, []
    for name in _INS:
        a = _np.ascontiguousarray(inputs[name])
        arrays[f"in_{name}_dram"] = a
        args.append(nc.dram_tensor(f"in_{name}_dram", a.shape, _mybir.dt.from_np(a.dtype), kind="ExternalInput").ap())
    for i, (shape, dtype) in enumerate(_OUTS):
        dt = _mybir.dt.from_np(_np.dtype(dtype))
        args.append(nc.dram_tensor(f"out_{i}_dram", shape, dt, kind="ExternalOutput").ap())
    gnn_resnorm_kernel(nc, *args)
    r = _run(nc, [arrays], core_ids=[0])
    got = tuple(r.results[0][f"out_{i}_dram"] for i in range(len(_OUTS)))
    return got[0]
```

```python
import concourse.bass as bass
from concourse import mybir
from contextlib import ExitStack

fp32 = mybir.dt.float32
bf16 = mybir.dt.bfloat16
f32r = mybir.dt.float32r
ALU = mybir.AluOpType
ACT = mybir.ActivationFunctionType
AX = mybir.AxisListType

P = 128
NEG = 9000000000000000.0
EPS = 1e-5
RING = 4


def gnn_resnorm_kernel(nc, x, adj, W, e, bias, out):
    B, N, F = x.shape
    T = N // P
    GB = 2
    NG = B // GB
    ROUNDS = NG // RING
    C = GB * F
    GC = T * C
    E = e.shape[1]
    CAP = 200

    x_v = x.rearrange("(n b) (p t) f -> n p b t f", b=GB, t=T)
    out_v = out.rearrange("(n b) (p t) f -> n p b t f", b=GB, t=T)

    ctx = ExitStack()
    with ctx:
        def sb(name, shape, dt=fp32):
            return ctx.enter_context(nc.sbuf_tensor(name, shape, dt))

        def ps(name, shape, dt=fp32):
            return ctx.enter_context(nc.psum_tensor(name, shape, dt))

        def sem(name):
            return ctx.enter_context(nc.semaphore(name))

        ident = sb("ident", [P, P])
        ident_b = sb("ident_b", [P, P], bf16)
        ones = sb("ones", [P, P])
        warm = sb("warm", [P, T * N], bf16)
        before = sb("before", [P, P])
        rank_row = sb("rank_row", [P, E])
        rank1_col = sb("rank1_col", [P, 1])
        eps_col = sb("eps_col", [P, 1])
        w_sb = sb("w_sb", [P, 2, F])
        w_diff = sb("w_diff", [P, F])
        bias_sb = sb("bias_sb", [P, 1, F])
        e_col = sb("e_col", [P, 1])
        e_last = sb("e_last", [P, 1])
        adj_sb = sb("adj_sb", [P, T * N])
        mask = sb("mask", [P, T * N])
        count = sb("count", [P, T * N])
        local = sb("local", [P, T * N], bf16)
        first = sb("first", [P, 1])
        first_b = sb("first_b", [P, 1], bf16)
        end = sb("end", [P, 1])
        thr = sb("thr", [P, 1])
        begun = sb("begun", [P, E])
        owner_t = sb("owner_t", [P, E], bf16)
        e_hi = sb("e_hi", [P, 1], f32r)
        e_lo = sb("e_lo", [P, 1])
        owner_hi = sb("owner_hi", [P, P], f32r)
        owner_lo = sb("owner_lo", [P, P], f32r)
        want = sb("want", [P, 1])
        placed = sb("placed", [P, T * N], f32r)
        late = sb("late", [P, T * N])
        off_edge = sb("off_edge", [P, T * N])
        neg_logit = sb("neg_logit", [P, T, N])
        neg_max = sb("neg_max", [P, T])
        ex = sb("ex", [P, T, N])
        rowsum = sb("rowsum", [P, T])
        rinv = sb("rinv", [P, T])
        diag_m = sb("diag_m", [P, T, P])
        diag_row = sb("diag_row", [P, T, P])
        at_hi = sb("at_hi", [P, T, T, P], f32r)
        at_lo = sb("at_lo", [P, T, T, P], f32r)
        xs = [sb(f"xs{k}", [P, GB, T, F]) for k in range(RING)]
        xb = sb("xb", [P, NG, GB, T, F])
        ys = [sb(f"ys{k}", [P, GB, T, F]) for k in range(RING)]
        xt = [sb(f"xt{k}", [P, GB, T, P]) for k in range(RING)]
        h_hi = [sb(f"h_hi{k}", [P, T, GB, F], f32r) for k in range(RING)]
        h_lo = [sb(f"h_lo{k}", [P, T, GB, F], f32r) for k in range(RING)]
        zs = [sb(f"zs{k}", [P, GB, T, P]) for k in range(2)]
        ts = [sb(f"ts{k}", [P, T, GB, F]) for k in range(RING)]
        stats = [sb(f"stats{k}", [P, T * GB, 6]) for k in range(2)]
        mv = [sb(f"mv{k}", [P, T * GB, 2]) for k in range(2)]
        std = [sb(f"std{k}", [P, T * GB]) for k in range(2)]
        rstd = [sb(f"rstd{k}", [P, T * GB]) for k in range(2)]
        shift = [sb(f"shift{k}", [P, T * GB]) for k in range(2)]

        ps_x = [ps(f"ps_x{k}", [P, GB, T, P]) for k in range(2)]
        ps_h = [ps(f"ps_h{k}", [P, T, GB, F]) for k in range(2)]
        ps_o = [ps(f"ps_o{k}", [P, T, GB, F]) for k in range(2)]
        ps_a = ps("ps_a", [P, T * N])
        ps_b = ps("ps_b", [P, T * N])
        owner_ps = ps_b[:, P:P + P // 2].bitcast(bf16)

        x_in = [sem(f"x_in{k}") for k in range(RING)]
        y_stored = [sem(f"y_stored{k}") for k in range(RING)]
        adj_in, w_in, bias_in, e_in = sem("adj_in"), sem("w_in"), sem("bias_in"), sem("e_in")
        warm_ok = sem("warm_ok")
        zeroed, consts, w_diff_ok = sem("zeroed"), sem("consts"), sem("w_diff_ok")
        mask_ok, count_ok, local_ok = sem("mask_ok"), sem("count_ok"), sem("local_ok")
        first_ps_ok, first_ok, thr_ok = sem("first_ps_ok"), sem("first_ok"), sem("thr_ok")
        begun_ok, owner_t_ok, owner_ps_ok = sem("begun_ok"), sem("owner_t_ok"), sem("owner_ps_ok")
        owner_ok, want_ok, placed_ok, sparse_ok = sem("owner_ok"), sem("want_ok"), sem("placed_ok"), sem("sparse_ok")
        e_neg_ok, off_edge_ok, late_ok, logit_ok = sem("e_neg_ok"), sem("off_edge_ok"), sem("late_ok"), sem("logit_ok")
        max_ok, exp_ok, rinv_ok = sem("max_ok"), sem("exp_ok"), sem("rinv_ok")
        diag_ok, diag_ps_ok, diag_row_ok = sem("diag_ok"), sem("diag_ps_ok"), sem("diag_row_ok")
        at_ps_ok, at_hi_ok, at_lo_ok = sem("at_ps_ok"), sem("at_hi_ok"), sem("at_lo_ok")
        xt_done, xt_ready = sem("xt_done"), sem("xt_ready")
        h_done, h_hi_ok, h_lo_ok = sem("h_done"), sem("h_hi_ok"), sem("h_lo_ok")
        biased, z_ready, mixed, summed = sem("biased"), sem("z_ready"), sem("mixed"), sem("summed")
        bn_done, var_ok, std_ok, rstd_ok, shift_ok = sem("bn_done"), sem("var_ok"), sem("std_ok"), sem("rstd_ok"), sem("shift_ok")
        normed_s, normed_v = sem("normed_s"), sem("normed_v")

        block = ctx.enter_context(nc.Block())

        def wait_count(eng, signal, count):
            if not isinstance(count, int) or count > 0:
                eng.wait_ge(signal, count)

        SOLO = (NG - 5, NG - 4, NG - 3)

        def alone(g):
            return isinstance(g, int) and g in SOLO

        MIX, SUM, ROOT, NORM = 3, 4, 5, 6
        WARM = 8
        SCALE, BIAS = MIX - 1, 0
        PEEL = 2

        @block.sync
        def _(sp):
            def load(g, k):
                wait_count(sp, xt_done, g - RING + 1)
                wait_count(sp, biased, g - RING + 1)
                sp.dma_start(xs[k][:, :, :, :], x_v[g]).then_inc(x_in[k], 16)

            def store(g, k):
                sp.wait_ge(normed_s, g + 1)
                if not alone(g):
                    after_solo = len(SOLO) if isinstance(g, int) and g > SOLO[-1] else 0
                    sp.wait_ge(normed_v, g + (1 - after_solo))
                sp.dma_start(out_v[g], ys[k][:, :, :, :]).then_inc(y_stored[k], 16)

            sp.dma_start(adj_sb[:, :], adj.rearrange("(p t) j -> p (t j)", t=T)).then_inc(adj_in, 16)
            for g in range(1, RING):
                load(g, g)
            for k in range(RING):
                sp.sem_inc(y_stored[k], 16)
            for g in range(RING, 2 * RING):
                load(g, g % RING)
            with sp.Fori(1, ROUNDS - 1) as r:
                g = r * RING
                for k in range(RING):
                    load(g + (RING + k), k)
                    store(g + (k - RING), k)
            for g in range(NG - 2 * RING, NG - 1):
                store(g, g % RING)
            sp.wait_ge(normed_s, NG)
            sp.dma_start(out_v[NG - 1][:, 0:GB - 1], ys[RING - 1][:, 0:GB - 1, :, :]).then_inc(y_stored[RING - 1], 16)
            sp.wait_ge(normed_v, NG - len(SOLO))
            sp.dma_start(out_v[NG - 1][:, GB - 1:GB], ys[RING - 1][:, GB - 1:GB, :, :]).then_inc(y_stored[RING - 1], 16)
            for k in range(RING):
                sp.wait_ge(y_stored[k], 16 * (ROUNDS + 1 + (k == RING - 1)))

        @block.gpsimd
        def _(pool):
            pool.memset(ident[:, :], 0.0).then_inc(zeroed, 1)
            pool.memset(before[:, :], 0.0).then_inc(zeroed, 1)
            pool.wait_ge(zeroed, 2)
            pool.affine_select(out=ident[:, :], in_=ident[:, :], compare_op=ALU.not_equal, fill=1.0,
                               base=0, pattern=[[-1, P]], channel_multiplier=1).then_inc(consts, 1)
            pool.affine_select(out=before[:, :], in_=before[:, :], compare_op=ALU.is_ge, fill=1.0,
                               base=0, pattern=[[-1, P]], channel_multiplier=1).then_inc(consts, 1)
            pool.iota(rank_row[:, :], pattern=[[1, E]], base=0, channel_multiplier=0,
                      allow_small_or_imprecise_dtypes=True).then_inc(consts, 1)
            pool.iota(rank1_col[:, :], pattern=[[1, 1]], base=1, channel_multiplier=1,
                      allow_small_or_imprecise_dtypes=True).then_inc(consts, 1)
            pool.wait_ge(consts, 1)
            pool.tensor_copy(ident_b[:, :], ident[:, :]).then_inc(consts, 1)
            pool.memset(ones[:, :], 1.0).then_inc(consts, 1)
            pool.memset(eps_col[:, :], EPS).then_inc(consts, 1)
            pool.wait_ge(w_in, 16)
            pool.tensor_tensor(w_diff[:, :], w_sb[:, 0, :], w_sb[:, 1, :], ALU.subtract).then_inc(w_diff_ok, 1)

            def add_bias(g, k, rounds):
                pool.wait_ge(x_in[k], rounds * 16 + 16)
                pool.tensor_tensor(xb[:, g, :, :, :].rearrange("p b t f -> p (b t) f"),
                                   xs[k][:, :, :, :].rearrange("p b t f -> p (b t) f"),
                                   bias_sb[:, :, :].broadcast_to([P, GB * T, F]), ALU.add).then_inc(biased, 1)

            def scale_by_diagonal(g, k):
                pool.wait_ge(xt_ready, g + 1)
                wait_count(pool, mixed, g - 1)
                pool.tensor_tensor(zs[k % 2][:, :, :, :].rearrange("p b t n -> p b (t n)"),
                                   xt[k][:, :, :, :].rearrange("p b t n -> p b (t n)"),
                                   diag_row[:, :, :].rearrange("p t n -> p (t n)").unsqueeze(1).broadcast_to([P, GB, T * P]),
                                   ALU.mult).then_inc(z_ready, 1)

            pool.wait_ge(bias_in, 16)
            for g in range(RING):
                add_bias(g, g, 0)
            pool.wait_ge(diag_row_ok, 1)
            for s in range(SCALE, RING + BIAS):
                scale_by_diagonal(s - SCALE, (s - SCALE) % RING)
            with pool.Fori(1, ROUNDS) as r:
                g = r * RING
                for k in range(RING):
                    scale_by_diagonal(g + (k + BIAS - SCALE), (k + BIAS - SCALE) % RING)
                    add_bias(g + k, k, r)
            for s in range(NG + BIAS, NG + SCALE):
                scale_by_diagonal(s - SCALE, (s - SCALE) % RING)

        @block.scalar
        def _(act):
            act.dma_start(xs[0][:, :, :, :], x_v[0]).then_inc(x_in[0], 16)
            act.dma_start(e_col[:, :], e.rearrange("a k -> k a")).then_inc(e_in, 16)
            act.dma_start(e_last[:, :], e[0:1, E - 1:E].broadcast_to([P, 1])).then_inc(e_in, 16)
            act.dma_start(w_sb[:, :, :], W.rearrange("w f g -> f w g")).then_inc(w_in, 16)
            act.dma_start(bias_sb[:, 0, :], bias.rearrange("(a f) -> a f", a=1).broadcast_to([P, F])).then_inc(bias_in, 16)

            def copy_xt(g, k):
                act.wait_ge(xt_done, g + 1)
                wait_count(act, h_done, g - RING + 1)
                wait_count(act, z_ready, g - RING + 1)
                act.activation(xt[k][:, :, :, :], ps_x[k % 2][:, :, :, :], ACT.Copy).then_inc(xt_ready, 1)

            def copy_h_hi(g, k):
                act.wait_ge(h_done, g + 1)
                wait_count(act, mixed, g - RING + 1)
                act.activation(h_hi[k][:, :, :, :], ps_h[k % 2][:, :, :, :], ACT.Copy).then_inc(h_hi_ok, 1)

            def deviation(g, k):
                act.wait_ge(var_ok, g + 1)
                wait_count(act, rstd_ok, g - 1)
                act.activation(std[k % 2][:, :], mv[k % 2][:, :, 1], ACT.Sqrt,
                               bias=eps_col[:, :], scale=1.0).then_inc(std_ok, 1)

            def normalise(g, k, rounds):
                act.wait_ge(shift_ok, g + 1)
                act.wait_ge(y_stored[k], rounds * 16 + 16)
                for b in range(GB if alone(g) else GB - 1):
                    for t in range(T):
                        j = t * GB + b
                        ins = act.activation(ys[k][:, b, t, :], ts[k][:, t, b, :], ACT.Identity,
                                             bias=shift[k % 2][:, j:j + 1], scale=rstd[k % 2][:, j:j + 1])
                ins.then_inc(normed_s, 1)

            for g in range(3):
                copy_xt(g, g)
            copy_h_hi(0, 0)
            copy_xt(3, 3)
            act.wait_ge(max_ok, 1)
            for t in range(T):
                act.activation(ex[:, t, :], neg_logit[:, t, :], ACT.Exp, bias=neg_max[:, t:t + 1], scale=-1.0,
                               accum_out=rowsum[:, t:t + 1]).then_inc(exp_ok, 1)
            copy_h_hi(1, 1)
            act.wait_ge(at_ps_ok, 1)
            act.activation(at_hi[:, :, :, :].rearrange("p s t n -> p (s t n)"), ps_a[:, :], ACT.Copy).then_inc(at_hi_ok, 1)
            act.wait_ge(diag_ps_ok, 1)
            act.activation(diag_row[:, :, :].rearrange("p t n -> p (t n)"), ps_b[:, 0:T * P], ACT.Copy).then_inc(diag_row_ok, 1)
            copy_h_hi(2, 2)
            copy_h_hi(3, 3)
            act.wait_ge(consts, 7)

            def step(s, k, rounds):
                if not isinstance(s, int) or ROOT <= s < NG + ROOT:
                    deviation(s - ROOT, (k - ROOT) % RING)
                if not isinstance(s, int) or s < NG:
                    copy_xt(s, k)
                if not isinstance(s, int) or RING < s <= NG:
                    copy_h_hi(s - 1, (k - 1) % RING)
                if not isinstance(s, int) or s >= NORM:
                    normalise(s - NORM, (k - NORM) % RING, rounds)

            for s in range(RING, PEEL * RING):
                step(s, s % RING, (s - NORM) // RING)
            with act.Fori(PEEL, ROUNDS) as r:
                for k in range(RING):
                    step(r * RING + k, k, r + (k - NORM) // RING)
            for s in range(NG, NG + NORM):
                step(s, s % RING, (s - NORM) // RING)

        @block.tensor
        def _(pe):
            def transposes(g, k, rounds):
                pe.wait_ge(x_in[k], rounds * 16 + 16)
                wait_count(pe, xt_ready, g - 1)
                for b in range(GB):
                    for t in range(T):
                        ins = pe.transpose(ps_x[k % 2][:, b, t, :], xs[k][:, b, t, :], ident[:, :])
                ins.then_inc(xt_done, 1)

            def h_products(g, k):
                pe.wait_ge(xt_ready, g + 1)
                wait_count(pe, h_lo_ok, g - 1)
                for b in range(GB):
                    for t in range(T):
                        ins = pe.matmul(ps_h[k % 2][:, t, b, :], xt[k][:, b, t, :], w_sb[:, 1, :], start=True, stop=True)
                ins.then_inc(h_done, 1)

            def mix(g, k):
                pe.wait_ge(h_lo_ok, g + 1)
                wait_count(pe, summed, g - 1)
                if isinstance(g, int) and g == 0:
                    pe.wait_ge(at_hi_ok, 1)
                    pe.wait_ge(at_lo_ok, 1)
                for t in range(T):
                    for s in range(T):
                        for n, (a, h) in enumerate(((at_hi, h_hi), (at_hi, h_lo), (at_lo, h_hi))):
                            pe.matmul(ps_o[k % 2][:, t, :, :], a[:, s, t, :], h[k][:, s, :, :],
                                      start=(t == 0 and s == 0 and n == 0), stop=False, skip_group_check=True)
                pe.wait_ge(z_ready, g + 1)
                for b in range(GB):
                    for t in range(T):
                        ins = pe.matmul(ps_o[k % 2][:, t, b, :], zs[k % 2][:, b, t, :], w_diff[:, :],
                                        start=False, stop=True, skip_group_check=True)
                ins.then_inc(mixed, 1)

            pe.wait_ge(warm_ok, 1)
            for _ in range(WARM):
                pe.matmul(ps_a[:, :], warm[:, 0:P], warm[:, :], start=True, stop=True)
            pe.wait_ge(consts, 6)
            pe.wait_ge(count_ok, 1)
            pe.matmul(ps_a[:, 0:1], before[:, :], count[:, T * N - 1:T * N], start=True, stop=True).then_inc(first_ps_ok, 1)
            transposes(0, 0, 0)
            transposes(1, 1, 0)
            pe.wait_ge(owner_t_ok, 1)
            pe.transpose(owner_ps, owner_t[:, :], ident_b[:, :]).then_inc(owner_ps_ok, 1)
            pe.wait_ge(first_ok, 3)
            pe.matmul(ps_b[:, 0:1], owner_t[:, :], first_b[:, :], start=True, stop=True).then_inc(owner_ps_ok, 1)
            pe.wait_ge(local_ok, 1)
            pe.matmul(ps_a[:, :], owner_t[:, :], local[:, :], start=True, stop=True).then_inc(owner_ps_ok, 1)
            pe.wait_ge(w_in, 16)
            h_products(0, 0)
            transposes(2, 2, 0)
            pe.wait_ge(owner_ok, 2)
            pe.wait_ge(placed_ok, 1)
            pe.matmul(ps_b[:, :], owner_hi[:, :], placed[:, :], start=True, stop=False)
            pe.matmul(ps_b[:, :], owner_lo[:, :], placed[:, :], start=False, stop=True).then_inc(sparse_ok, 1)
            transposes(3, 3, 0)
            h_products(1, 1)
            transposes(RING, 0, 1)
            h_products(2, 2)
            pe.wait_ge(exp_ok, T)
            for s in range(T):
                for t in range(T):
                    ins = pe.transpose(ps_a[:, (s * T + t) * P:(s * T + t + 1) * P], ex[:, t, s:N:T], ident[:, :])
            ins.then_inc(at_ps_ok, 1)
            pe.wait_ge(diag_ok, T)
            pe.matmul(ps_b[:, 0:T * P], ones[:, :], diag_m[:, :, :], start=True, stop=True).then_inc(diag_ps_ok, 1)
            h_products(3, 3)
            pe.wait_ge(w_diff_ok, 1)
            for s in range(MIX, RING):
                mix(s - MIX, s - MIX)
            for s in range(RING, PEEL * RING):
                if s > RING:
                    transposes(s, s % RING, 1)
                    h_products(s - 1, (s - 1) % RING)
                mix(s - MIX, (s - MIX) % RING)
            with pe.Fori(PEEL, ROUNDS) as r:
                g = r * RING
                for k in range(RING):
                    transposes(g + k, k, r)
                    h_products(g + (k - 1), (k - 1) % RING)
                    mix(g + (k - MIX), (k - MIX) % RING)
            h_products(NG - 1, RING - 1)
            for g in range(NG - MIX, NG):
                mix(g, g % RING)

        @block.vector
        def _(dve):
            dve.memset(warm[:, :], 0.0).then_inc(warm_ok, 1)
            dve.wait_ge(adj_in, 16)
            dve.tensor_scalar(mask[:, :], adj_sb[:, :], 0.0, None, ALU.is_gt).then_inc(mask_ok, 1)
            dve.wait_ge(mask_ok, 1)
            dve.tensor_tensor_scan(count[:, :], mask[:, :], mask[:, :], 0.0, ALU.add, ALU.max).then_inc(count_ok, 1)
            dve.wait_ge(count_ok, 1)
            dve.scalar_tensor_tensor(local[:, :], count[:, :], float(CAP), mask[:, :], ALU.min, ALU.mult).then_inc(local_ok, 1)
            dve.tensor_scalar(off_edge[:, :], mask[:, :], -NEG, NEG, ALU.mult, ALU.add).then_inc(off_edge_ok, 1)
            dve.wait_ge(first_ps_ok, 1)
            dve.tensor_copy(first[:, :], ps_a[:, 0:1]).then_inc(first_ok, 1)
            dve.wait_ge(first_ok, 1)
            dve.tensor_tensor(end[:, :], first[:, :], count[:, T * N - 1:T * N], ALU.add).then_inc(first_ok, 1)
            dve.tensor_scalar(begun[:, :], rank_row[:, :], first[:, :], None, ALU.is_ge).then_inc(begun_ok, 1)
            dve.tensor_copy(first_b[:, :], first[:, :]).then_inc(first_ok, 1)
            dve.wait_ge(first_ok, 3)
            dve.wait_ge(begun_ok, 1)
            dve.scalar_tensor_tensor(owner_t[:, :], rank_row[:, :], end[:, :], begun[:, :], ALU.is_lt, ALU.mult).then_inc(owner_t_ok, 1)
            dve.tensor_scalar(thr[:, :], first[:, :], -1.0, float(E), ALU.mult, ALU.add).then_inc(thr_ok, 1)
            dve.wait_ge(e_in, 32)
            dve.tensor_scalar(e_last[:, :], e_last[:, :], -1.0, None, ALU.mult).then_inc(e_neg_ok, 1)
            dve.tensor_scalar(e_hi[:, :], e_col[:, :], -1.0, None, ALU.mult).then_inc(e_neg_ok, 1)
            dve.wait_ge(e_neg_ok, 2)
            dve.scalar_tensor_tensor(e_lo[:, :], e_col[:, :], -1.0, e_hi[:, :].bitcast(fp32), ALU.mult, ALU.subtract).then_inc(e_neg_ok, 1)
            dve.wait_ge(thr_ok, 1)
            dve.scalar_tensor_tensor(late[:, :], count[:, :], thr[:, :], mask[:, :], ALU.is_gt, ALU.mult).then_inc(late_ok, 1)
            dve.wait_ge(owner_ps_ok, 3)
            dve.tensor_tensor(want[:, :], rank1_col[:, :], ps_b[:, 0:1], ALU.subtract).then_inc(want_ok, 1)
            dve.wait_ge(e_neg_ok, 3)
            dve.tensor_scalar(owner_hi[:, :], owner_ps, e_hi[:, :].bitcast(fp32), None, ALU.mult).then_inc(owner_ok, 1)
            dve.tensor_scalar(owner_lo[:, :], owner_ps, e_lo[:, :], None, ALU.mult).then_inc(owner_ok, 1)
            dve.wait_ge(want_ok, 1)
            dve.tensor_scalar(placed[:, :], ps_a[:, :], want[:, :], None, ALU.is_equal).then_inc(placed_ok, 1)
            dve.wait_ge(late_ok, 1)
            dve.wait_ge(off_edge_ok, 1)
            dve.scalar_tensor_tensor(late[:, :], late[:, :], e_last[:, :], off_edge[:, :], ALU.mult, ALU.add).then_inc(late_ok, 1)
            dve.wait_ge(late_ok, 2)
            dve.wait_ge(sparse_ok, 1)
            dve.tensor_tensor(neg_logit[:, :, :].rearrange("p t n -> p (t n)"), ps_b[:, :], late[:, :], ALU.add).then_inc(logit_ok, 1)
            dve.wait_ge(logit_ok, 1)
            dve.tensor_reduce(neg_max[:, :], neg_logit[:, :, :], AX.X, ALU.min).then_inc(max_ok, 1)

            def split_h_lo(g, k):
                dve.wait_ge(h_hi_ok, g + 1)
                wait_count(dve, mixed, g - RING + 1)
                dve.tensor_tensor(h_lo[k][:, :, :, :], ps_h[k % 2][:, :, :, :], h_hi[k][:, :, :, :].bitcast(fp32),
                                  ALU.subtract).then_inc(h_lo_ok, 1)

            def add_residual(g, k):
                dve.wait_ge(mixed, g + 1)
                dve.wait_ge(biased, g + 1)
                wait_count(dve, normed_s, g - RING + 1)
                for t in range(T):
                    ins = dve.scalar_tensor_tensor(ts[k][:, t, :, :], ps_o[k % 2][:, t, :, :], rinv[:, t:t + 1],
                                                   xb[:, g, :, t, :], ALU.mult, ALU.add)
                ins.then_inc(summed, 1)

            def statistics(g, k):
                dve.wait_ge(summed, g + 1)
                for t in range(T):
                    for b in range(GB):
                        ins = dve.bn_stats(stats[k % 2][:, t * GB + b, :], ts[k][:, t, b, :])
                ins.then_inc(bn_done, 1)

            def invert(g, k):
                dve.wait_ge(std_ok, g + 1)
                wait_count(dve, normed_s, g - 1)
                dve.reciprocal(rstd[k % 2][:, :], std[k % 2][:, :]).then_inc(rstd_ok, 1)

            def aggregate(g, k):
                for j in range(T * GB):
                    ins = dve.bn_aggr(mv[k % 2][:, j, :], stats[k % 2][:, j, :])
                ins.then_inc(var_ok, 1)

            def shifts(g, k):
                dve.wait_ge(rstd_ok, g + 1)
                dve.scalar_tensor_tensor(shift[k % 2][:, :], mv[k % 2][:, :, 0], -1.0, rstd[k % 2][:, :],
                                         ALU.mult, ALU.mult).then_inc(shift_ok, 1)

            def normalise(g, k, rounds):
                dve.wait_ge(y_stored[k], rounds * 16 + 16)
                b = GB - 1
                for t in range(T):
                    j = t * GB + b
                    ins = dve.tensor_scalar(ys[k][:, b, t, :], ts[k][:, t, b, :], mv[k % 2][:, j, 0:1],
                                            rstd[k % 2][:, j:j + 1], ALU.subtract, ALU.mult)
                ins.then_inc(normed_v, 1)

            split_h_lo(0, 0)
            dve.wait_ge(exp_ok, T)
            for t in range(T):
                dve.tensor_tensor(diag_m[:, t, :], ex[:, t, t:N:T], ident[:, :], ALU.mult).then_inc(diag_ok, 1)
            dve.reciprocal(rinv[:, :], rowsum[:, :]).then_inc(rinv_ok, 1)
            split_h_lo(1, 1)
            dve.wait_ge(at_hi_ok, 1)
            dve.tensor_tensor(at_lo[:, :, :, :].rearrange("p s t n -> p (s t n)"), ps_a[:, :],
                              at_hi[:, :, :, :].rearrange("p s t n -> p (s t n)").bitcast(fp32),
                              ALU.subtract).then_inc(at_lo_ok, 1)
            dve.wait_ge(rinv_ok, 1)

            def step(s, k, rounds):
                looped = not isinstance(s, int)
                summing = looped or SUM <= s < NG + SUM
                scaling = looped or ROOT <= s < NG + ROOT
                if summing:
                    add_residual(s - SUM, (k - SUM) % RING)
                if scaling:
                    invert(s - ROOT, (k - ROOT) % RING)
                if summing:
                    statistics(s - SUM, (k - SUM) % RING)
                if scaling:
                    shifts(s - ROOT, (k - ROOT) % RING)
                draining = not looped and s > NG
                if summing:
                    dve.wait_ge(bn_done, s - SUM + 1)
                if summing and draining:
                    aggregate(s - SUM, (k - SUM) % RING)
                if scaling and not alone(s - ROOT):
                    normalise(s - ROOT, (k - ROOT) % RING, rounds)
                if looped or s <= NG:
                    split_h_lo(s - 1, (k - 1) % RING)
                if summing and not draining:
                    aggregate(s - SUM, (k - SUM) % RING)

            for s in range(RING - 1, PEEL * RING):
                step(s, s % RING, (s - ROOT) // RING)
            with dve.Fori(PEEL, ROUNDS) as r:
                for k in range(RING):
                    step(r * RING + k, k, r + (k - ROOT) // RING)
            for s in range(NG, NG + ROOT):
                step(s, s % RING, (s - ROOT) // RING)


_INS = ['x', 'adj', 'L0_gnn_W', 'L0_gnn_e', 'L0_gnn_bias']
_OUTS = [((32, 256, 128), 'float32')]


def kernel(**inputs):
    import numpy as _np
    import concourse.bacc as _bacc
    from concourse import mybir as _mybir
    from concourse.bass_utils import run_bass_kernel_spmd as _run

    nc = _bacc.Bacc("TRN2", target_bir_lowering=False, num_devices=1)
    arrays, args = {}, []
    for name in _INS:
        a = _np.ascontiguousarray(inputs[name])
        arrays[f"in_{name}_dram"] = a
        args.append(nc.dram_tensor(f"in_{name}_dram", a.shape, _mybir.dt.from_np(a.dtype), kind="ExternalInput").ap())
    for i, (shape, dtype) in enumerate(_OUTS):
        dt = _mybir.dt.from_np(_np.dtype(dtype))
        args.append(nc.dram_tensor(f"out_{i}_dram", shape, dt, kind="ExternalOutput").ap())
    gnn_resnorm_kernel(nc, *args)
    r = _run(nc, [arrays], core_ids=[0])
    got = tuple(r.results[0][f"out_{i}_dram"] for i in range(len(_OUTS)))
    return got[0]
```
